# Optimizing a Trainium2 kernel written in Bass

```python
import numpy as np
import jax
import jax.numpy as jnp

def _softmax(x, axis=-1):
    return jax.nn.softmax(x, axis=axis)
def _gelu(x):
    return jax.nn.gelu(x, approximate=True)
def _silu(x):
    return jax.nn.silu(x)
def _sigmoid(x):
    return jax.nn.sigmoid(x)
def _layernorm(x, axis=-1, eps=1e-5):
    m = jnp.mean(x, axis=axis, keepdims=True)
    v = jnp.var(x, axis=axis, keepdims=True)
    return (x - m) / jnp.sqrt(v + eps)
def _scatter_add(tgt, idx, src, axis=0):
    return tgt.at[idx].add(src)
def _segment_sum(src, seg, n):
    return jax.ops.segment_sum(src, seg, n)

kernel_name = 'mk_adj_preln_d4_adj_256_78054d'

def setup_inputs(seed: int = 0):
    np.random.seed(seed)
    _w = jnp.asarray
    def _rec_inputs():
        import jax
        import jax.numpy as jnp
        _gk = jax.random.key(seed)
        x = -0.0002928 + 1 * jax.random.normal(jax.random.fold_in(_gk, 1), (32, 512, 256), jnp.float32)
        _a = jax.random.bernoulli(jax.random.fold_in(_gk, 2), 0.0078125, (32, 512, 512))
        _a = jnp.logical_or(_a, jnp.swapaxes(_a, -1, -2))
        _a = jnp.logical_or(_a, jnp.eye(512, dtype=bool))
        adj = _a.astype(jnp.int32)
        return x, adj
    x, adj = _rec_inputs()
    def _L0_gnn_setup():
        import jax, jax.numpy as jnp
        import numpy as np
        NEG_BIG = -9000000000000000.0
        key = jax.random.key(seed)
        k1, k2, k3, k4 = jax.random.split(key, 4)
        B, N, F_in, F_out = (4, 4096, 256, 256)
        h = jax.random.normal(k1, (B, N, F_in), dtype=jnp.float32)
        adj = jax.random.randint(k2, (B, N, N), 0, 2, dtype=jnp.int32)
        bW = 1.414 * np.sqrt(6.0 / (F_in + F_out))
        W = jax.random.uniform(k3, (F_in, F_out), minval=-bW, maxval=bW, dtype=jnp.float32)
        ba = 1.414 * np.sqrt(6.0 / (2 * F_out + 1))
        a = jax.random.uniform(k4, (2 * F_out, 1), minval=-ba, maxval=ba, dtype=jnp.float32)
        return {'h': h, 'adj': adj, 'W': W, 'a': a}
    _L0_gnn_all = _L0_gnn_setup()
    _L0_gnn_in = {k: v for k, v in _L0_gnn_all.items() if k in ('W', 'a', )}
    del _L0_gnn_all

    def _L1_gnn_setup():
        import jax, jax.numpy as jnp
        import numpy as np
        NEG_INF = -1000000000.0
        LEAKY_SLOPE = 0.2
        key = jax.random.key(seed)
        k1, k2, k3, k4 = jax.random.split(key, 4)
        B, N, D_in, D_out = (8, 2048, 256, 256)
        x = jax.random.normal(k1, (B, N, D_in), dtype=jnp.float32)
        adj_matrix = jax.random.randint(k2, (B, N, N), 0, 2, dtype=jnp.int32)
        W = jax.random.normal(k3, (D_out, D_in), dtype=jnp.float32) / np.sqrt(D_in)
        a = jax.random.normal(k4, (1, 2 * D_out), dtype=jnp.float32) / np.sqrt(2 * D_out)
        return {'x': x, 'adj_matrix': adj_matrix, 'W': W, 'a': a}
    _L1_gnn_all = _L1_gnn_setup()
    _L1_gnn_in = {k: v for k, v in _L1_gnn_all.items() if k in ('W', 'a', )}
    del _L1_gnn_all

    def _L2_gnn_setup():
        import jax, jax.numpy as jnp
        import numpy as np
        BS, N, D, R = (16, 512, 256, 2)
        key = jax.random.key(seed)
        ks = jax.random.split(key, 9)
        s = 1.0 / np.sqrt(D)
        return {'encoded_spans': jax.random.normal(ks[0], (BS, N, D), dtype=jnp.float32), 'w_rel1': jax.random.normal(ks[1], (R, D, D), dtype=jnp.float32) * s, 'w_root1': jax.random.normal(ks[2], (D, D), dtype=jnp.float32) * s, 'b1': jnp.zeros((D,), dtype=jnp.float32), 'w_rel2': jax.random.normal(ks[3], (R, D, D), dtype=jnp.float32) * s, 'w_root2': jax.random.normal(ks[4], (D, D), dtype=jnp.float32) * s, 'b2': jnp.zeros((D,), dtype=jnp.float32), 'aug_adj': jax.random.randint(ks[5], (BS, N, N), 0, 16, dtype=jnp.int64), 'punct_graph': jax.random.randint(ks[6], (BS, N, N), 0, 16, dtype=jnp.int64)}
    _L2_gnn_all = _L2_gnn_setup()
    _L2_gnn_in = {k: v for k, v in _L2_gnn_all.items() if k in ('w_rel1', 'w_root1', 'b1', 'w_rel2', 'w_root2', 'b2', )}
    del _L2_gnn_all

    def _L3_gnn_setup():
        import jax, jax.numpy as jnp
        import numpy as np
        B, N, F_IN, F_OUT = (8, 2048, 256, 256)
        ALPHA = 0.2
        NEG_BIG = -9000000000000000.0
        key = jax.random.key(seed)
        k1, k2, k3, k4 = jax.random.split(key, 4)
        x = jax.random.normal(k1, (B, N, F_IN), dtype=jnp.float32)
        adj = jax.random.randint(k2, (B, N, N), 0, 2, dtype=jnp.int32)
        gain = 1.414
        lim_W = gain * np.sqrt(6.0 / (F_IN + F_OUT))
        W = jax.random.uniform(k3, (F_IN, F_OUT), dtype=jnp.float32, minval=-lim_W, maxval=lim_W)
        lim_a = gain * np.sqrt(6.0 / (2 * F_OUT + 1))
        a = jax.random.uniform(k4, (2 * F_OUT, 1), dtype=jnp.float32, minval=-lim_a, maxval=lim_a)
        return {'x': x, 'adj': adj, 'W': W, 'a': a}
    _L3_gnn_all = _L3_gnn_setup()
    _L3_gnn_in = {k: v for k, v in _L3_gnn_all.items() if k in ('W', 'a', )}
    del _L3_gnn_all

    return {
        "x": x,
        "adj": adj,
        "L0_gnn_W": _L0_gnn_in["W"],
        "L0_gnn_a": _L0_gnn_in["a"],
        "L1_gnn_W": _L1_gnn_in["W"],
        "L1_gnn_a": _L1_gnn_in["a"],
        "L2_gnn_w_rel1": _L2_gnn_in["w_rel1"],
        "L2_gnn_w_root1": _L2_gnn_in["w_root1"],
        "L2_gnn_b1": _L2_gnn_in["b1"],
        "L2_gnn_w_rel2": _L2_gnn_in["w_rel2"],
        "L2_gnn_w_root2": _L2_gnn_in["w_root2"],
        "L2_gnn_b2": _L2_gnn_in["b2"],
        "L3_gnn_W": _L3_gnn_in["W"],
        "L3_gnn_a": _L3_gnn_in["a"],
    }

def reference(x, adj, L0_gnn_W, L0_gnn_a, L1_gnn_W, L1_gnn_a, L2_gnn_w_rel1, L2_gnn_w_root1, L2_gnn_b1, L2_gnn_w_rel2, L2_gnn_w_root2, L2_gnn_b2, L3_gnn_W, L3_gnn_a):
    import jax
    import jax.numpy as jnp
    def _L0_gnn_ref(h, adj, W, a):
        import jax, jax.numpy as jnp
        import numpy as np
        NEG_BIG = -9000000000000000.0
        F_out = W.shape[1]
        Wh = jnp.einsum('bnf,fo->bno', h, W)
        src = Wh @ a[:F_out, 0]
        dst = Wh @ a[F_out:, 0]
        e = jax.nn.leaky_relu(src[:, :, None] + dst[:, None, :], negative_slope=0.2)
        scores = jnp.where(adj > 0, e, jnp.float32(NEG_BIG))
        attention = jax.nn.softmax(scores, axis=2)
        h_prime = jnp.einsum('bij,bjo->bio', attention, Wh)
        return jax.nn.relu(h_prime)

    def _L1_gnn_ref(x, adj_matrix, W, a):
        import jax, jax.numpy as jnp
        import numpy as np
        NEG_INF = -1000000000.0
        LEAKY_SLOPE = 0.2
        h = jnp.einsum('bnd,od->bno', x, W)
        D = h.shape[-1]
        a_left, a_right = (a[0, :D], a[0, D:])
        e = (h @ a_left)[:, :, None] + (h @ a_right)[:, None, :]
        e = jnp.where(e > 0, e, LEAKY_SLOPE * e)
        e = jnp.where(adj_matrix == 0, NEG_INF, e)
        alpha = jax.nn.softmax(e, axis=-1)
        return jnp.einsum('bij,bjd->bid', alpha, h)

    def _L2_gnn_ref(encoded_spans, w_rel1, w_root1, b1, w_rel2, w_root2, b2, aug_adj, punct_graph):
        import jax, jax.numpy as jnp
        import numpy as np
        BS, N, D, R = (16, 512, 256, 2)
        mask_punct = (punct_graph == 1) & (aug_adj != 1)
        mask_aug = aug_adj == 1
        masks = jnp.stack([mask_punct, mask_aug]).astype(encoded_spans.dtype)
        deg = jnp.maximum(masks.sum(axis=2), 1.0)[..., None]

        def conv(x, w_rel, w_root, b):
            out = jnp.einsum('bnd,de->bne', x, w_root) + b
            for r in range(R):
                agg = jnp.einsum('bij,bid->bjd', masks[r], x) / deg[r]
                out = out + jnp.einsum('bjd,de->bje', agg, w_rel[r])
            return out
        h = jax.nn.elu(conv(encoded_spans, w_rel1, w_root1, b1))
        h = jax.nn.elu(conv(h, w_rel2, w_root2, b2))
        return h

    def _L3_gnn_ref(x, adj, W, a):
        import jax, jax.numpy as jnp
        import numpy as np
        B, N, F_IN, F_OUT = (8, 2048, 256, 256)
        ALPHA = 0.2
        NEG_BIG = -9000000000000000.0
        h = jnp.einsum('bnf,fo->bno', x, W)
        a1 = a[:F_OUT, 0]
        a2 = a[F_OUT:, 0]
        s1 = h @ a1
        s2 = h @ a2
        e = jax.nn.leaky_relu(s1[:, :, None] + s2[:, None, :], negative_slope=ALPHA)
        att = jnp.where(adj > 0, e, jnp.float32(NEG_BIG))
        att = jax.nn.softmax(att, axis=1)
        h_prime = jnp.einsum('bij,bjo->bio', att, h)
        return jax.nn.elu(h_prime)

    h = jnp.maximum(_layernorm(x, axis=-1), 0.0)
    x = x + _L0_gnn_ref(h, adj, L0_gnn_W, L0_gnn_a)
    h = jnp.maximum(_layernorm(x, axis=-1), 0.0)
    x = x + _L1_gnn_ref(h, adj, L1_gnn_W, L1_gnn_a)
    h = jnp.maximum(_layernorm(x, axis=-1), 0.0)
    x = x + _L2_gnn_ref(h, L2_gnn_w_rel1, L2_gnn_w_root1, L2_gnn_b1, L2_gnn_w_rel2, L2_gnn_w_root2, L2_gnn_b2, adj, adj)
    h = jnp.maximum(_layernorm(x, axis=-1), 0.0)
    x = x + _L3_gnn_ref(h, adj, L3_gnn_W, L3_gnn_a)
    return x


_drawn_inputs = setup_inputs


def setup_inputs(seed=0):
    import zlib

    import numpy as np

    out = dict(_drawn_inputs(seed))
    spreads = {'L2_gnn_b1': (0.0, 0.1), 'L2_gnn_b2': (0.0, 0.1)}
    factors = {}
    for name, (base, spread) in spreads.items():
        noise = np.random.default_rng([zlib.crc32(name.encode()), seed]).standard_normal(out[name].shape)
        drawn = base * np.exp(spread * noise) if base else spread * noise
        out[name] = jnp.asarray(drawn.astype(out[name].dtype))
    for name, factor in factors.items():
        out[name] = (out[name] * factor).astype(out[name].dtype)
    return out
```

```python
from contextlib import ExitStack

import concourse.bass as bass
from concourse import mybir

F32 = mybir.dt.float32
F32R = mybir.dt.float32r
BF16 = mybir.dt.bfloat16
I32 = mybir.dt.int32
ALU = mybir.AluOpType
ACT = mybir.ActivationFunctionType

P = 128
SLOTS = 2
MASKED = -(2.0 ** 53)
SLOPE = 0.2
EPS = 1e-5
LOWEST = -3.0e38
GAT_OF_LAYER = {0: 0, 1: 1, 3: 2}


def interleave(*programs):
    programs = list(programs)
    while programs:
        for program in list(programs):
            try:
                next(program)
            except StopIteration:
                programs.remove(program)


def build(nc, x, adj, gat_w, gat_a, conv_rel, conv_root, conv_bias, out):
    B, N, D = x.shape
    T = N // P
    K = D // P
    ROUNDS = B // SLOTS
    WS = D + 2
    DMA = 16

    ctx = ExitStack()
    with ctx:
        def sb(name, shape, dt=F32):
            return ctx.enter_context(nc.sbuf_tensor(name, shape, dt))

        def slots(name, shape, dt=F32):
            return [sb(f"{name}_{s}", shape, dt) for s in range(SLOTS)]

        def sem(name):
            return ctx.enter_context(nc.semaphore(name))

        def sems(name):
            return [sem(f"{name}_{s}") for s in range(SLOTS)]

        adj_raw = slots("adj_raw", [P, T, N], I32)
        kind = slots("kind", [P, T, N], BF16)
        pen = slots("pen", [P, T, N], BF16)
        pen_turned = slots("pen_turned", [P, T, N], BF16)
        edge = slots("edge", [P, T, N], F32R)
        xs = slots("xs", [P, T, D])
        h = slots("h", [P, T, D])
        h_hi = slots("h_hi", [P, T, D], F32R)
        h_lo = slots("h_lo", [P, T, D], F32R)
        ht_hi = slots("ht_hi", [P, K, N], F32R)
        ht_lo = slots("ht_lo", [P, K, N], F32R)
        score = slots("score", [P, T, N])
        prob = slots("prob", [P, T, N])
        pt_hi = slots("pt_hi", [P, T, T, P], F32R)
        pt_lo = slots("pt_lo", [P, T, T, P], F32R)
        result = [score[s][:, :, D:2 * D] for s in range(SLOTS)]
        stats = slots("stats", [P, T, 6])
        mean_var = slots("mean_var", [P, T, 2])
        var_eps = slots("var_eps", [P, T])
        rstd = slots("rstd", [P, T])
        mean_rstd = slots("mean_rstd", [P, T])
        neg_mean_rstd = slots("neg_mean_rstd", [P, T])
        sd = slots("sd", [P, T, 2])
        own_slope = slots("own_slope", [P, T])
        other_max = slots("other_max", [P, T])
        neg_top = slots("neg_top", [P, T])
        neg_max = slots("neg_max", [P, T])
        row_sum = slots("row_sum", [P, T])
        inv_sum = slots("inv_sum", [P, T])
        degree = slots("degree", [P, T])
        inv_degree = slots("inv_degree", [P, T])
        wg_hi = [sb(f"wg_hi_{i}", [P, K, WS], F32R) for i in range(3)]
        wg_lo = [sb(f"wg_lo_{i}", [P, K, WS], F32R) for i in range(3)]
        wc_hi = [sb(f"wc_hi_{i}", [P, K, D], F32R) for i in range(4)]
        wc_lo = [sb(f"wc_lo_{i}", [P, K, D], F32R) for i in range(4)]
        bias_hi = sb("bias_hi", [1, 2, D], F32R)
        bias_lo = sb("bias_lo", [1, 2, D], F32R)
        wa = sb("wa", [P, 3, K, 2])
        ident = sb("ident", [P, P])
        ident16 = sb("ident16", [P, P], BF16)
        ones_row = sb("ones_row", [1, P], F32R)
        ones_col = sb("ones_col", [P, 2], F32R)
        settled = sb("settled", [P, 1])
        eps_t = sb("eps_t", [P, T])
        half_t = sb("half_t", [P, T])
        zero_t = sb("zero_t", [P, T])

        ps = [ctx.enter_context(nc.psum_tensor(f"ps_{s}", [P, T, 512], F32)) for s in range(SLOTS)]
        assert T == 4 and K == 2 and D == 256 and N == 512

        weights_in = sem("weights_in")
        consts = sem("consts")
        w1_turned = sem("w1_turned")
        wa_done = sem("wa_done")
        w_hi_done = sem("w_hi_done")
        weights_ready = sem("weights_ready")
        def sems_of(**events_per_graph):
            return [sems(name) for name in events_per_graph]

        x_in, adj_in, out_stored, kind_ready, pen_ready, edge_ready = sems_of(
            x_in=DMA, adj_in=DMA, out_stored=DMA, kind_ready=1, pen_ready=2, edge_ready=1)
        pent_ps, pent_ready, deg_ps, deg_ready, stats_ready, mv_ready = sems_of(
            pent_ps=1, pent_ready=1, deg_ps=1, deg_ready=2, stats_ready=4, mv_ready=4)
        ln_step, h_ready, ht_ps, hth_ready, htl_ready, wh_ps = sems_of(
            ln_step=16, h_ready=16, ht_ps=5, hth_ready=5, htl_ready=5, wh_ps=3)
        whh_ready, whl_ready, sd_ready, bc_ps, q_ready, slope_ready = sems_of(
            whh_ready=3, whl_ready=3, sd_ready=3, bc_ps=3, q_ready=12, slope_ready=12)
        r_ready, p_ready, inv_ready, own_slope_ready, max_step, pt_ps = sems_of(
            r_ready=12, p_ready=12, inv_ready=12, own_slope_ready=3, max_step=6, pt_ps=8)
        pth_ready, ptl_ready, att_ps, relu_ready, elu_exp, elu_clamped = sems_of(
            pth_ready=12, ptl_ready=12, att_ps=12, relu_ready=4, elu_exp=4, elu_clamped=8)
        elu_ready, x_ready, hh_ready, hl_ready, agg_ps, agh_ready = sems_of(
            elu_ready=6, x_ready=16, hh_ready=2, hl_ready=2, agg_ps=4, agh_ready=4)
        agl_ready, root_ps, root_ready, rel_ps, u_ready, ce_ready = sems_of(
            agl_ready=4, root_ps=4, root_ready=4, rel_ps=4, u_ready=4, ce_ready=4)
        (h1_ready,) = sems_of(
            h1_ready=2)

        def first(n):
            return isinstance(n, int) and n == 0

        def split3(pe, acc, pairs, last_stop=True, first=True):
            for i, (lh, ll, rh, rl) in enumerate(pairs):
                pe.matmul(acc, lh, rh, start=(first and i == 0), stop=False)
                pe.matmul(acc, lh, rl, start=False, stop=False)
                mm = pe.matmul(acc, ll, rh, start=False, stop=(last_stop and i == len(pairs) - 1))
            return mm

        def raw(i):
            tile = score[1] if i < 4 else prob[1]
            return tile[:, i % 4, :].rearrange("p (k o) -> p k o", k=K)

        W0, W1_RAW, W3, ROOT1, REL1, ROOT2, REL2, W1 = range(8)
        vectors = prob[0]
        bias_raw = prob[0][0:1, 3, :].rearrange("q (c d) -> q c d", c=2)
        scratch = h[1]

        block = ctx.enter_context(nc.Block())

        @block.sync
        def _(sp):
            def load_adj(s, n):
                sp.dma_start(adj_raw[s][:], adj[SLOTS * n + s].rearrange("(t p) j -> p t j", p=P))\
                    .then_inc(adj_in[s], DMA)

            def load_x(s, n):
                sp.dma_start(xs[s][:], x[SLOTS * n + s].rearrange("(t p) d -> p t d", p=P))\
                    .then_inc(x_in[s], DMA)

            def store(s, n):
                sp.wait_ge(x_ready[s], 16 * n + 16)
                sp.dma_start(out[SLOTS * n + s].rearrange("(t p) d -> p t d", p=P), result[s])\
                    .then_inc(out_stored[s], DMA)

            load_adj(0, 0)
            load_x(0, 0)
            for i, w in enumerate((gat_w[0], gat_w[1], gat_w[2], conv_root[0], conv_rel[0][1],
                                   conv_root[1], conv_rel[1][1])):
                sp.dma_start(raw(i), w.rearrange("(k p) o -> p k o", p=P)).then_inc(weights_in, DMA)
            for i, a in enumerate(gat_a):
                sp.dma_start(vectors[:, i, :], a.rearrange("(q a) b -> q (a b)", q=1).to_broadcast([P, 2 * D]))\
                    .then_inc(weights_in, DMA)
            for c in range(2):
                sp.dma_start(bias_raw[:, c, :], conv_bias[c].rearrange("(q d) -> q d", q=1))\
                    .then_inc(weights_in, DMA)
            load_adj(1, 0)
            load_x(1, 0)
            with sp.Fori(0, ROUNDS - 1) as n:
                for s in range(SLOTS):
                    sp.wait_ge(kind_ready[s], n + 1)
                    load_adj(s, n + 1)
                for s in range(SLOTS):
                    store(s, n)
                    load_x(s, n + 1)
            for s in range(SLOTS):
                store(s, ROUNDS - 1)
            for s in range(SLOTS):
                sp.wait_ge(out_stored[s], DMA * ROUNDS)

        def run(eng, gat, conv):
            interleave(gat(0, 0, 0))
            interleave(gat(0, 1, 0))
            interleave(conv(0, 0), gat(1, 0, 0))
            interleave(gat(0, 3, 0), gat(1, 1, 0))
            with eng.Fori(1, ROUNDS) as n:
                interleave(gat(0, 0, n), conv(1, n - 1))
                interleave(gat(0, 1, n), gat(1, 3, n - 1))
                interleave(conv(0, n), gat(1, 0, n))
                interleave(gat(0, 3, n), gat(1, 1, n))
            interleave(conv(1, ROUNDS - 1))
            interleave(gat(1, 3, ROUNDS - 1))

        @block.gpsimd
        def _(pool):
            pool.memset(ident[:], 0.0).then_inc(consts, 1)
            pool.memset(ident16[:], 0.0).then_inc(consts, 1)
            pool.memset(ones_row[:].bitcast(F32), 1.0).then_inc(consts, 1)
            pool.memset(ones_col[:].bitcast(F32), 1.0).then_inc(consts, 1)
            pool.memset(eps_t[:], EPS).then_inc(consts, 1)
            pool.memset(half_t[:], -0.5).then_inc(consts, 1)
            pool.memset(zero_t[:], 0.0).then_inc(consts, 1)
            pool.wait_ge(consts, 7)
            for m in (ident, ident16):
                pool.affine_select(out=m[:], in_=m[:], compare_op=ALU.not_equal, fill=1.0, base=0,
                                   pattern=[[-1, P]], channel_multiplier=1).then_inc(consts, 1)

            def layernorm_columns(s, layer, n):
                k = 4 * layer
                pool.wait_ge(mv_ready[s], 4 * n + layer + 1)
                pool.tensor_tensor(var_eps[s][:], mean_var[s][:, :, 1], eps_t[:], ALU.add).then_inc(ln_step[s], 1)
                pool.wait_ge(ln_step[s], 16 * n + k + 1)
                pool.tensor_tensor(rstd[s][:], var_eps[s][:], half_t[:], ALU.pow).then_inc(ln_step[s], 1)
                pool.wait_ge(ln_step[s], 16 * n + k + 2)
                pool.tensor_tensor(mean_rstd[s][:], mean_var[s][:, :, 0], rstd[s][:], ALU.mult)\
                    .then_inc(ln_step[s], 1)
                pool.wait_ge(ln_step[s], 16 * n + k + 3)
                pool.tensor_tensor(neg_mean_rstd[s][:], zero_t[:], mean_rstd[s][:], ALU.subtract)\
                    .then_inc(ln_step[s], 1)

            def gat(s, layer, n):
                layernorm_columns(s, layer, n)
                for _ in range(20):
                    yield

            def conv(s, n):
                layernorm_columns(s, 2, n)
                for _ in range(20):
                    yield

            run(pool, gat, conv)

        TILE_STEPS = [("prob", 0), ("prob", 1), ("prob", 2), ("split", 0), ("prob", 3), ("split", 1),
                      ("out", 0), ("split", 2), ("out", 1), ("split", 3), ("out", 2), ("out", 3)]
        TILE_STEPS_3 = [("prob", 0), ("prob", 1), ("split", 0), ("prob", 2), ("split", 1), ("prob", 3),
                        ("split", 2), ("split", 3), ("out", 0), ("out", 1), ("out", 2), ("out", 3)]

        @block.scalar
        def _(act):
            act.wait_ge(consts, 9)

            def normalise(s, layer, n):
                act.wait_ge(ln_step[s], 16 * n + 4 * layer + 4)
                for t in range(T):
                    act.activation(h[s][:, t, :], xs[s][:, t, :], ACT.Relu, scale=rstd[s][:, t:t + 1],
                                   bias=neg_mean_rstd[s][:, t:t + 1]).then_inc(h_ready[s], 1)

            def turned_hi(s, turn, n):
                act.wait_ge(ht_ps[s], 5 * n + turn + 1)
                act.activation(ht_hi[s][:], ps[s][:, 0:K, :], ACT.Copy).then_inc(hth_ready[s], 1)

            def gat(s, layer, n):
                g = GAT_OF_LAYER[layer]
                turn = {0: 0, 1: 1, 3: 4}[layer]
                normalise(s, layer, n)
                if layer == 0:
                    act.wait_ge(pent_ps[s], n + 1)
                    act.activation(pen_turned[s][:], ps[s][:, 2:4, :].bitcast(BF16).rearrange(
                        "p b (t i) -> p (b t) i", t=2), ACT.Copy).then_inc(pent_ready[s], 1)
                yield
                turned_hi(s, turn, n)
                yield
                yield
                act.wait_ge(wh_ps[s], 3 * n + g + 1)
                act.activation(h_hi[s][:], ps[s][:, :, 0:D], ACT.Copy).then_inc(whh_ready[s], 1)
                yield
                for t in range(T):
                    act.wait_ge(own_slope_ready[s], 3 * n + g + 1)
                    act.wait_ge(q_ready[s], 12 * n + 4 * g + t + 1)
                    act.activation(prob[s][:, t, :], score[s][:, t, :], ACT.Identity, scale=SLOPE,
                                   bias=own_slope[s][:, t:t + 1]).then_inc(slope_ready[s], 1)
                    yield
                for what, t in TILE_STEPS_3 if layer == 3 else TILE_STEPS:
                    if what == "prob":
                        if t == 0:
                            act.wait_ge(max_step[s], 6 * n + 2 * g + 2)
                        act.wait_ge(r_ready[s], 12 * n + 4 * g + t + 1)
                        act.activation(prob[s][:, t, :], score[s][:, t, :], ACT.Exp,
                                       bias=neg_max[s][:, t:t + 1], accum_out=row_sum[s][:, t:t + 1])\
                            .then_inc(p_ready[s], 1)
                    elif what == "split":
                        if layer == 3:
                            act.wait_ge(inv_ready[s], 12 * n + 4 * g + t + 1)
                            act.activation(pt_hi[s][:, t, :, :].rearrange("p a b -> p (a b)"), prob[s][:, t, :],
                                           ACT.Copy, scale=inv_sum[s][:, t:t + 1]).then_inc(pth_ready[s], 1)
                        else:
                            act.wait_ge(pt_ps[s], 8 * n + 4 * g + t + 1)
                            act.activation(pt_hi[s][:, t, :, :].rearrange("p a b -> p (a b)"), ps[s][:, t, :],
                                           ACT.Copy).then_inc(pth_ready[s], 1)
                    elif layer == 0:
                        act.wait_ge(inv_ready[s], 12 * n + 4 * g + t + 1)
                        act.wait_ge(att_ps[s], 12 * n + 4 * g + t + 1)
                        act.activation(score[s][:, t, 0:D], ps[s][:, t, 0:D], ACT.Relu,
                                       scale=inv_sum[s][:, t:t + 1]).then_inc(relu_ready[s], 1)
                    elif layer == 3:
                        act.wait_ge(att_ps[s], 12 * n + 4 * g + t + 1)
                        act.activation(score[s][:, t, 0:D], ps[s][:, t, 0:D], ACT.Exp)\
                            .then_inc(elu_exp[s], 1)
                    yield

            def conv(s, n):
                for c in range(2):
                    if c == 0:
                        normalise(s, 2, n)
                        act.wait_ge(h_ready[s], 16 * n + 12)
                    else:
                        act.wait_ge(h1_ready[s], 2 * n + 2)
                    act.activation(h_hi[s][:], h[s][:], ACT.Copy).then_inc(hh_ready[s], 1)
                    yield
                    turned_hi(s, 2 + c, n)
                    yield
                    yield
                    for k in range(K):
                        act.wait_ge(agg_ps[s], 4 * n + 2 * c + k + 1)
                        act.activation(pt_hi[s][:, k, :, :].rearrange("p a b -> p (a b)"), ps[s][:, 2 + k, :],
                                       ACT.Copy).then_inc(agh_ready[s], 1)
                        yield
                    for half in range(2):
                        act.wait_ge(root_ps[s], 4 * n + 2 * c + half + 1)
                        act.activation(score[s][:, half, :], ps[s][:, half, :], ACT.Copy)\
                            .then_inc(root_ready[s], 1)
                        yield
                    for half in range(2):
                        act.wait_ge(u_ready[s], 4 * n + 2 * c + half + 1)
                        act.activation(prob[s][:, half, :], score[s][:, 2 + half, :], ACT.Exp)\
                            .then_inc(ce_ready[s], 1)
                        yield
                    yield

            run(act, gat, conv)

        @block.vector
        def _(dve):
            dve.wait_ge(weights_in, 12 * DMA)
            dve.wait_ge(w1_turned, 1)
            dve.tensor_copy(raw(W1), ps[0][:, 0:K, 0:D]).then_inc(wa_done, 1)
            dve.wait_ge(wa_done, 1)
            count = 1
            for g, w in enumerate((W0, W1, W3)):
                for k in range(K):
                    for c in range(2):
                        dve.tensor_tensor_reduce(scratch[:, 0, :], raw(w)[:, k, :], vectors[:, g, c * D:(c + 1) * D],
                                                 1.0, 0.0, ALU.mult, ALU.add, wa[:, g, k, c:c + 1])\
                            .then_inc(wa_done, 1)
                        count += 1
                        dve.wait_ge(wa_done, count)
            splits = []
            for g, w in enumerate((W0, W1, W3)):
                splits.append((wg_hi[g][:, :, 0:D], wg_lo[g][:, :, 0:D], raw(w)))
                splits.append((wg_hi[g][:, :, D:WS], wg_lo[g][:, :, D:WS], wa[:, g, :, :]))
            for i, w in enumerate((ROOT1, REL1, ROOT2, REL2)):
                splits.append((wc_hi[i][:], wc_lo[i][:], raw(w)))
            splits.append((bias_hi[:], bias_lo[:], bias_raw[:]))
            for hi, _, full in splits:
                dve.tensor_copy(hi, full).then_inc(w_hi_done, 1)
            dve.wait_ge(w_hi_done, len(splits))
            for hi, lo, full in splits:
                dve.tensor_tensor(lo, full, hi.bitcast(F32), ALU.subtract).then_inc(weights_ready, 1)
            assert len(splits) == N_SPLITS

            def layernorm(s, layer, n):
                if layer == 0:
                    dve.wait_ge(x_in[s], DMA * (n + 1))
                else:
                    dve.wait_ge(x_ready[s], 16 * n + 4 * layer)
                for t in range(T):
                    st = dve.bn_stats(stats[s][:, t, :], xs[s][:, t, :])
                st.then_inc(stats_ready[s], 1)
                dve.wait_ge(stats_ready[s], 4 * n + layer + 1)
                dve.memset(settled[:], 0.0)
                for t in range(T):
                    agg = dve.bn_aggr(mean_var[s][:, t, :], stats[s][:, t, :])
                agg.then_inc(mv_ready[s], 1)

            def turned_lo(s, turn, n):
                dve.wait_ge(hth_ready[s], 5 * n + turn + 1)
                dve.tensor_tensor(ht_lo[s][:], ps[s][:, 0:K, :], ht_hi[s][:].bitcast(F32), ALU.subtract)\
                    .then_inc(htl_ready[s], 1)

            def gat(s, layer, n):
                g = GAT_OF_LAYER[layer]
                turn = {0: 0, 1: 1, 3: 4}[layer]
                own = 1 if layer == 3 else 0
                if layer == 0:
                    dve.wait_ge(adj_in[s], DMA * (n + 1))
                    dve.tensor_scalar(kind[s][:], adj_raw[s][:], 2.0, -1.0, ALU.min, ALU.max)\
                        .then_inc(kind_ready[s], 1)
                    dve.wait_ge(kind_ready[s], n + 1)
                    dve.tensor_scalar(pen[s][:], kind[s][:], 0.0, MASKED, ALU.is_le, ALU.mult)\
                        .then_inc(pen_ready[s], 1)
                    layernorm(s, layer, n)
                    dve.tensor_scalar(edge[s][:], kind[s][:], 1.0, None, ALU.is_equal)\
                        .then_inc(edge_ready[s], 1)
                else:
                    layernorm(s, layer, n)
                if layer == 1:
                    dve.wait_ge(pent_ps[s], n + 1)
                    dve.wait_ge(q_ready[s], 12 * n + 4)
                    dve.tensor_scalar(pen[s][:], kind[s][:], 0.0, MASKED, ALU.is_equal, ALU.mult)\
                        .then_inc(pen_ready[s], 1)
                yield
                turned_lo(s, turn, n)
                yield
                yield
                dve.wait_ge(whh_ready[s], 3 * n + g + 1)
                dve.tensor_copy(sd[s][:], ps[s][:, :, D:WS]).then_inc(sd_ready[s], 1)
                dve.tensor_tensor(h_lo[s][:], ps[s][:, :, 0:D], h_hi[s][:].bitcast(F32), ALU.subtract)\
                    .then_inc(whl_ready[s], 1)
                yield
                penalties = pen_turned if layer == 3 else pen
                for t in range(T):
                    if t == 0:
                        dve.wait_ge(bc_ps[s], 3 * n + g + 1)
                        if layer == 3:
                            dve.wait_ge(pent_ready[s], n + 1)
                        else:
                            dve.wait_ge(pen_ready[s], 2 * n + g + 1)
                        if layer == 0:
                            if not first(n):
                                dve.wait_ge(out_stored[s], DMA * n)
                        dve.tensor_scalar(own_slope[s][:], sd[s][:, :, own], SLOPE, None, ALU.mult)\
                            .then_inc(own_slope_ready[s], 1)
                    dve.tensor_tensor_reduce(score[s][:, t, :], ps[s][:, T - 1, :], penalties[s][:, t, :],
                                             1.0, LOWEST, ALU.add, ALU.max, other_max[s][:, t:t + 1])\
                        .then_inc(q_ready[s], 1)
                    if t == T - 1:
                        dve.wait_ge(q_ready[s], 12 * n + 4 * g + 4)
                        dve.scalar_tensor_tensor(out=neg_top[s][:], in0=other_max[s][:], scalar=-1.0,
                                                 in1=sd[s][:, :, own], op0=ALU.mult, op1=ALU.subtract)\
                            .then_inc(max_step[s], 1)
                        dve.wait_ge(max_step[s], 6 * n + 2 * g + 1)
                        dve.scalar_tensor_tensor(out=neg_max[s][:], in0=neg_top[s][:], scalar=SLOPE,
                                                 in1=neg_top[s][:], op0=ALU.mult, op1=ALU.min)\
                            .then_inc(max_step[s], 1)
                    yield
                for what, t in TILE_STEPS_3 if layer == 3 else TILE_STEPS:
                    if what == "prob":
                        dve.wait_ge(slope_ready[s], 12 * n + 4 * g + t + 1)
                        dve.scalar_tensor_tensor(out=score[s][:, t, :], in0=score[s][:, t, :],
                                                 scalar=sd[s][:, t, own:own + 1], in1=prob[s][:, t, :],
                                                 op0=ALU.add, op1=ALU.max).then_inc(r_ready[s], 1)
                    elif what == "split":
                        dve.wait_ge(p_ready[s], 12 * n + 4 * g + t + 1)
                        dve.reciprocal(inv_sum[s][:, t:t + 1], row_sum[s][:, t:t + 1]).then_inc(inv_ready[s], 1)
                        hi = pt_hi[s][:, t, :, :].rearrange("p a b -> p (a b)").bitcast(F32)
                        lo = pt_lo[s][:, t, :, :].rearrange("p a b -> p (a b)")
                        dve.wait_ge(pth_ready[s], 12 * n + 4 * g + t + 1)
                        if layer == 3:
                            dve.scalar_tensor_tensor(out=lo, in0=prob[s][:, t, :], scalar=inv_sum[s][:, t:t + 1],
                                                     in1=hi, op0=ALU.mult, op1=ALU.subtract)\
                                .then_inc(ptl_ready[s], 1)
                        else:
                            dve.tensor_tensor(lo, ps[s][:, t, :], hi, ALU.subtract).then_inc(ptl_ready[s], 1)
                    elif layer == 0:
                        dve.wait_ge(relu_ready[s], 4 * n + t + 1)
                        dve.tensor_tensor(xs[s][:, t, :], xs[s][:, t, :], score[s][:, t, 0:D], ALU.add)\
                            .then_inc(x_ready[s], 1)
                    elif layer == 1:
                        dve.wait_ge(att_ps[s], 12 * n + 4 * g + t + 1)
                        dve.scalar_tensor_tensor(out=xs[s][:, t, :], in0=ps[s][:, t, 0:D],
                                                 scalar=inv_sum[s][:, t:t + 1], in1=xs[s][:, t, :],
                                                 op0=ALU.mult, op1=ALU.add).then_inc(x_ready[s], 1)
                    else:
                        e = score[s][:, t, 0:D]
                        dve.wait_ge(elu_exp[s], 4 * n + t + 1)
                        dve.tensor_scalar(e, e, 1.0, -1.0, ALU.min, ALU.add).then_inc(elu_clamped[s], 1)
                        dve.wait_ge(elu_clamped[s], 8 * n + 4 + t + 1)
                        dve.tensor_tensor(e, ps[s][:, t, 0:D], e, ALU.max).then_inc(elu_ready[s], 1)
                        dve.wait_ge(elu_ready[s], 6 * n + 2 + t + 1)
                        dve.tensor_tensor(result[s][:, t, :], xs[s][:, t, :], e, ALU.add)\
                            .then_inc(x_ready[s], 1)
                    yield

            def conv(s, n):
                for c in range(2):
                    if c == 0:
                        layernorm(s, 2, n)
                    yield
                    if c == 0:
                        dve.wait_ge(deg_ps[s], n + 1)
                        dve.tensor_scalar(degree[s][:], ps[s][:, 3, 0:2 * T].rearrange("p (t two) -> p t two", two=2)[:, :, 0],
                                          1.0, None, ALU.max).then_inc(deg_ready[s], 1)
                    dve.wait_ge(hh_ready[s], 2 * n + c + 1)
                    dve.tensor_tensor(h_lo[s][:], h[s][:], h_hi[s][:].bitcast(F32), ALU.subtract)\
                        .then_inc(hl_ready[s], 1)
                    turned_lo(s, 2 + c, n)
                    if c == 0:
                        dve.wait_ge(deg_ready[s], 2 * n + 1)
                        dve.reciprocal(inv_degree[s][:], degree[s][:]).then_inc(deg_ready[s], 1)
                    yield
                    yield
                    for k in range(K):
                        dve.wait_ge(agh_ready[s], 4 * n + 2 * c + k + 1)
                        dve.tensor_tensor(pt_lo[s][:, k, :, :].rearrange("p a b -> p (a b)"), ps[s][:, 2 + k, :],
                                          pt_hi[s][:, k, :, :].rearrange("p a b -> p (a b)").bitcast(F32),
                                          ALU.subtract).then_inc(agl_ready[s], 1)
                        yield
                    for half in range(2):
                        yield
                    for half in range(2):
                        dve.wait_ge(deg_ready[s], 2 * n + 2)
                        dve.wait_ge(root_ready[s], 4 * n + 2 * c + half + 1)
                        dve.wait_ge(rel_ps[s], 4 * n + 2 * c + half + 1)
                        for i in range(2):
                            t = 2 * half + i
                            u = dve.scalar_tensor_tensor(
                                out=score[s][:, 2 + half, i * D:(i + 1) * D], in0=ps[s][:, 2 + half, i * D:(i + 1) * D],
                                scalar=inv_degree[s][:, t:t + 1], in1=score[s][:, half, i * D:(i + 1) * D],
                                op0=ALU.mult, op1=ALU.add)
                        u.then_inc(u_ready[s], 1)
                        yield
                    for half in range(2):
                        e = prob[s][:, half, :]
                        dve.wait_ge(ce_ready[s], 4 * n + 2 * c + half + 1)
                        dve.tensor_scalar(e, e, 1.0, -1.0, ALU.min, ALU.add).then_inc(elu_clamped[s], 1)
                    for half in range(2):
                        e = prob[s][:, half, :]
                        u = score[s][:, 2 + half, :]
                        tiles = slice(2 * half, 2 * half + 2)
                        dve.wait_ge(elu_clamped[s], 8 * n + 2 * c + half + 1)
                        if c == 0:
                            dve.tensor_tensor(h[s][:, tiles, :].rearrange("p a b -> p (a b)"), u, e, ALU.max)\
                                .then_inc(h1_ready[s], 1)
                        else:
                            dve.tensor_tensor(e, u, e, ALU.max).then_inc(elu_ready[s], 1)
                            dve.wait_ge(elu_ready[s], 6 * n + half + 1)
                            for i in range(2):
                                t = 2 * half + i
                                dve.tensor_tensor(xs[s][:, t, :], xs[s][:, t, :], e[:, i * D:(i + 1) * D], ALU.add)\
                                    .then_inc(x_ready[s], 1)
                    yield

            run(dve, gat, conv)

        @block.tensor
        def _(pe):
            pe.wait_ge(consts, 9)
            pe.wait_ge(weights_in, 12 * DMA)
            for k in range(K):
                for o in range(K):
                    mm = pe.transpose(ps[0][:, k, o * P:(o + 1) * P], raw(W1_RAW)[:, o, k * P:(k + 1) * P], ident[:])
            mm.then_inc(w1_turned, 1)
            pe.wait_ge(weights_ready, N_SPLITS)

            def turn_h(s, turn, n, ready, event):
                for t in range(T):
                    if ready == "h_ready":
                        pe.wait_ge(h_ready[s], 16 * n + event + t)
                    elif t == 0:
                        pe.wait_ge(h1_ready[s], 2 * n + 2)
                    for k in range(K):
                        mm = pe.transpose(ps[s][:, k, t * P:(t + 1) * P], h[s][:, t, k * P:(k + 1) * P], ident[:])
                mm.then_inc(ht_ps[s], 1)

            def gat(s, layer, n):
                g = GAT_OF_LAYER[layer]
                turn = {0: 0, 1: 1, 3: 4}[layer]
                other = 0 if layer == 3 else 1
                if layer == 0:
                    pe.wait_ge(pen_ready[s], 2 * n + 1)
                    if not first(n):
                        pe.wait_ge(x_ready[s], 16 * n)
                    turned = ps[s][:, 2:4, :].bitcast(BF16).rearrange("p b (t i) -> p (b t) i", t=2)
                    for j in range(T):
                        for i in range(T):
                            mm = pe.transpose(turned[:, j, i * P:(i + 1) * P], pen[s][:, i, j * P:(j + 1) * P], ident16[:])
                    mm.then_inc(pent_ps[s], 1)
                turn_h(s, turn, n, "h_ready", 4 * layer + 1)
                yield
                yield
                pe.wait_ge(hth_ready[s], 5 * n + turn + 1)
                pe.wait_ge(htl_ready[s], 5 * n + turn + 1)
                if layer == 0:
                    pe.wait_ge(pent_ready[s], n + 1)
                for t in range(T):
                    c = slice(t * P, (t + 1) * P)
                    mm = split3(pe, ps[s][:, t, 0:WS],
                                [(ht_hi[s][:, k, c], ht_lo[s][:, k, c], wg_hi[g][:, k, :], wg_lo[g][:, k, :])
                                 for k in range(K)])
                mm.then_inc(wh_ps[s], 1)
                yield
                pe.wait_ge(sd_ready[s], 3 * n + g + 1)
                pe.wait_ge(whl_ready[s], 3 * n + g + 1)
                for t in range(T):
                    mm = pe.transpose(ps[s][:, T - 1, t * P:(t + 1) * P],
                                      sd[s][:, t, other:other + 1].to_broadcast([P, P]), ident[:])
                mm.then_inc(bc_ps[s], 1)
                yield
                for t in range(T):
                    yield

                def attention(t):
                    pairs = []
                    for j in range(T):
                        a, b = (j, t) if layer == 3 else (t, j)
                        pairs.append((pt_hi[s][:, a, b, :], pt_lo[s][:, a, b, :], h_hi[s][:, j, :], h_lo[s][:, j, :]))
                    split3(pe, ps[s][:, t, 0:D], pairs).then_inc(att_ps[s], 1)

                for what, t in TILE_STEPS_3 if layer == 3 else TILE_STEPS:
                    if what == "prob" and layer != 3:
                        pe.wait_ge(q_ready[s], 12 * n + 4 * g + 4)
                        pe.wait_ge(p_ready[s], 12 * n + 4 * g + t + 1)
                        for j in range(T):
                            mm = pe.transpose(ps[s][:, t, j * P:(j + 1) * P], prob[s][:, t, j * P:(j + 1) * P], ident[:])
                        mm.then_inc(pt_ps[s], 1)
                    elif what == "split" and layer != 3:
                        pe.wait_ge(pth_ready[s], 12 * n + 4 * g + t + 1)
                        pe.wait_ge(ptl_ready[s], 12 * n + 4 * g + t + 1)
                        attention(t)
                    elif what == "out" and layer == 3:
                        if t == 0:
                            pe.wait_ge(ptl_ready[s], 12 * n + 4 * g + 4)
                        attention(t)
                    yield

            def conv(s, n):
                for c in range(2):
                    if c == 0:
                        turn_h(s, 2, n, "h_ready", 9)
                        pe.wait_ge(edge_ready[s], n + 1)
                        pe.wait_ge(x_ready[s], 16 * n + 8)
                        for j in range(T):
                            for i in range(T):
                                mm = pe.matmul(ps[s][:, 3, 2 * j:2 * j + 2], edge[s][:, i, j * P:(j + 1) * P],
                                               ones_col[:], start=(i == 0), stop=(i == T - 1))
                        mm.then_inc(deg_ps[s], 1)
                    else:
                        turn_h(s, 3, n, "h1_ready", 2)
                    yield
                    yield
                    for k in range(K):
                        if k == 0:
                            pe.wait_ge(hh_ready[s], 2 * n + c + 1)
                            pe.wait_ge(hl_ready[s], 2 * n + c + 1)
                            pe.wait_ge(deg_ready[s], 2 * n + 1)
                        for i, part in enumerate((h_hi, h_lo)):
                            for t in range(T):
                                mm = pe.matmul(ps[s][:, 2 + k, :], part[s][:, t, k * P:(k + 1) * P], edge[s][:, t, :],
                                               start=(i == 0 and t == 0), stop=(i == 1 and t == T - 1))
                        mm.then_inc(agg_ps[s], 1)
                        yield
                    for half in range(2):
                        if half == 0:
                            pe.wait_ge(hth_ready[s], 5 * n + 3 + c)
                            pe.wait_ge(htl_ready[s], 5 * n + 3 + c)
                        for i in range(2):
                            t = 2 * half + i
                            cols = slice(t * P, (t + 1) * P)
                            acc = ps[s][:, half, i * D:(i + 1) * D]
                            split3(pe, acc, [(ht_hi[s][:, k, cols], ht_lo[s][:, k, cols],
                                              wc_hi[2 * c][:, k, :], wc_lo[2 * c][:, k, :]) for k in range(K)],
                                   last_stop=False)
                            pe.matmul(acc, ones_row[:], bias_hi[:, c, :], start=False, stop=False)
                            mm = pe.matmul(acc, ones_row[:], bias_lo[:, c, :], start=False, stop=True)
                        mm.then_inc(root_ps[s], 1)
                        yield
                    for half in range(2):
                        if half == 0:
                            pe.wait_ge(agh_ready[s], 4 * n + 2 * c + 2)
                            pe.wait_ge(agl_ready[s], 4 * n + 2 * c + 2)
                        for i in range(2):
                            t = 2 * half + i
                            mm = split3(pe, ps[s][:, 2 + half, i * D:(i + 1) * D],
                                        [(pt_hi[s][:, k, t, :], pt_lo[s][:, k, t, :],
                                          wc_hi[2 * c + 1][:, k, :], wc_lo[2 * c + 1][:, k, :]) for k in range(K)])
                        mm.then_inc(rel_ps[s], 1)
                        yield
                    yield

            run(pe, gat, conv)


N_SPLITS = 11


_INS = ["x", "adj", "L0_gnn_W", "L0_gnn_a", "L1_gnn_W", "L1_gnn_a", "L2_gnn_w_rel1", "L2_gnn_w_root1",
        "L2_gnn_b1", "L2_gnn_w_rel2", "L2_gnn_w_root2", "L2_gnn_b2", "L3_gnn_W", "L3_gnn_a"]


def kernel(**inputs):
    import numpy as _np
    import concourse.bacc as _bacc
    from concourse.bass_utils import run_bass_kernel_spmd as _run

    nc = _bacc.Bacc("TRN2", target_bir_lowering=False, num_devices=1)
    arrays, a = {}, {}
    for name in _INS:
        v = _np.ascontiguousarray(inputs[name])
        arrays[name] = v
        a[name] = nc.dram_tensor(name, v.shape, mybir.dt.from_np(v.dtype), kind="ExternalInput").ap()
    out = nc.dram_tensor("out", inputs["x"].shape, F32, kind="ExternalOutput").ap()
    build(nc, a["x"], a["adj"], [a["L0_gnn_W"], a["L1_gnn_W"], a["L3_gnn_W"]],
          [a["L0_gnn_a"], a["L1_gnn_a"], a["L3_gnn_a"]],
          [a["L2_gnn_w_rel1"], a["L2_gnn_w_rel2"]], [a["L2_gnn_w_root1"], a["L2_gnn_w_root2"]],
          [a["L2_gnn_b1"], a["L2_gnn_b2"]], out)
    r = _run(nc, [arrays], core_ids=[0])
    return r.results[0]["out"]
```

```python
from contextlib import ExitStack

import concourse.bass as bass
from concourse import mybir

F32 = mybir.dt.float32
F32R = mybir.dt.float32r
BF16 = mybir.dt.bfloat16
I32 = mybir.dt.int32
ALU = mybir.AluOpType
ACT = mybir.ActivationFunctionType

P = 128
SLOTS = 2
MASKED = -(2.0 ** 53)
SLOPE = 0.2
EPS = 1e-5
LOWEST = -3.0e38
GAT_OF_LAYER = {0: 0, 1: 1, 3: 2}
N_SPLITS = 11


SEGMENTS = ["front", "rows", "front", "rows", "norm", "conv", "conv", "front", "columns"]
WORDS = dict(v="values", s="score", e="exp", c="copy", p="product", o="out")
ROWS = "v0 v1 s0 v2 s1 e0 v3 s2 e1 c0 p0 s3 e2 c1 p1 e3 c2 o0 c3 p2 o1 p3 o2 o3".split()
COLUMNS = "v0 v1 s0 v2 s1 e0 v3 s2 e1 c0 s3 e2 c1 e3 c2 c3 p0 p1 o0 p2 o1 p3 o2 o3".split()
BACK_STEPS = {layer: [(WORDS[w[0]], int(w[1])) for w in steps] for layer, steps in
              {0: ROWS, 1: ROWS, 3: COLUMNS}.items()}
PLAN = [
    [0, 0.5, 4.2, 18.4, 18.4, 19.3],
    [23.0, 24.0, 24.2, 24.4, 24.4, 30.8, 32.2, 32.2, 34.9, 34.9, 40.9, 42.3, 42.9, 42.9, 42.9, 42.9,
     42.9, 42.9, 42.9, 42.9, 42.9, 45.4, 45.4, 46.4],
    [46.5, 47.4, 47.9, 49.2, 50.3, 50.8],
    [50.8, 50.8, 50.8, 50.8, 50.8, 52.0, 52.0, 52.3, 54.4, 55.6, 61.0, 61.0, 61.0, 61.0, 61.0, 61.0,
     61.0, 61.8, 63.9, 65.4, 65.4, 65.4, 65.6, 66.1],
    [67.4, 67.4],
    [67.4, 67.9, 74.6, 81.1, 81.1, 83.0, 92.2, 92.2, 92.5],
    [94.1, 94.1, 99.6, 108.2, 108.8, 109.5, 109.5, 109.5, 111.0],
    [111.0, 112.1, 120.0, 121.5, 122.7, 124.8],
    [126.1, 127.4, 128.3, 128.4, 130.4, 131.4, 135.4, 135.4, 136.9, 136.9, 137.1, 137.1, 137.1, 139.6,
     140.4, 140.4, 140.8, 141.1, 142.7, 144.2, 148.6, 148.6, 148.6, 148.6],
]
PERIOD = 150.0
BEHIND = 75.0
HALFWAY = 5


def interleave(*programs):
    turns = sorted((round(at, 1), which) for which, (_, times) in enumerate(programs) for at in times)
    for _, which in turns:
        next(programs[which][0])
    for program, _ in programs:
        assert next(program, "over") == "over"


def build(nc, x, adj, gat_w, gat_a, conv_rel, conv_root, conv_bias, out):
    B, N, D = x.shape
    T = N // P
    K = D // P
    ROUNDS = B // SLOTS
    WS = D + 4
    OWN, OTHER, OWN_SLOPE = D, D + 1, D + 2
    DMA = 16

    ctx = ExitStack()
    with ctx:
        def sb(name, shape, dt=F32):
            return ctx.enter_context(nc.sbuf_tensor(name, shape, dt))

        def slots(name, shape, dt=F32):
            return [sb(f"{name}_{s}", shape, dt) for s in range(SLOTS)]

        def sem(name):
            return ctx.enter_context(nc.semaphore(name))

        def sems(name):
            return [sem(f"{name}_{s}") for s in range(SLOTS)]

        adj_raw = slots("adj_raw", [P, T, N], I32)
        pen = slots("pen", [P, T, N], BF16)
        pen_turned = slots("pen_turned", [P, T, N], BF16)
        edge = slots("edge", [P, T, N], F32R)
        x_new = slots("x_new", [P, T, D])
        xs = slots("xs", [P, T, D])
        h = slots("h", [P, T, WS])
        h_hi = slots("h_hi", [P, T, D], F32R)
        h_lo = slots("h_lo", [P, T, D], F32R)
        ht_hi = slots("ht_hi", [P, K, N], F32R)
        ht_lo = slots("ht_lo", [P, K, N], F32R)
        score = slots("score", [P, T, N])
        prob = slots("prob", [P, T, N])
        turned_prob = slots("turned_prob", [P, T, N])
        sum_hi = slots("sum_hi", [P, K, N], F32R)
        sum_lo = slots("sum_lo", [P, K, N], F32R)
        result = [score[s][:, :, D:2 * D] for s in range(SLOTS)]
        stats = slots("stats", [P, T, 6])
        mean_var = slots("mean_var", [P, T, 2])
        var_eps = slots("var_eps", [P, T])
        rstd = slots("rstd", [P, T])
        neg_max = slots("neg_max", [P, T])
        row_sum = slots("row_sum", [P, T])
        inv_sum = slots("inv_sum", [P, T])
        degree = slots("degree", [P, T])
        inv_degree = slots("inv_degree", [P, T])
        wg_hi = [sb(f"wg_hi_{i}", [P, K, WS], F32R) for i in range(3)]
        wg_lo = [sb(f"wg_lo_{i}", [P, K, WS], F32R) for i in range(3)]
        wc_hi = [sb(f"wc_hi_{i}", [P, K, D], F32R) for i in range(4)]
        wc_lo = [sb(f"wc_lo_{i}", [P, K, D], F32R) for i in range(4)]
        bias_hi = sb("bias_hi", [1, 2, D], F32R)
        bias_lo = sb("bias_lo", [1, 2, D], F32R)
        wa = sb("wa", [P, 3, K, 4])
        half_t = sb("half_t", [P, T])
        ident = sb("ident", [P, P])
        ident16 = sb("ident16", [P, P], BF16)
        ones_row = sb("ones_row", [1, P], F32R)
        ones_col = sb("ones_col", [P, 2], F32R)
        settled = sb("settled", [P, 1])

        ps = [ctx.enter_context(nc.psum_tensor(f"ps_{s}", [P, T, 512], F32)) for s in range(SLOTS)]
        assert T == 4 and K == 2 and D == 256 and N == 512
        BANK = (3, 0, 1, 2)

        def other(s):
            return turned_prob[s][:, T - 1, :]


        def turned(s, half):
            return ps[s][:, half, :].rearrange("p (k n) -> p k n", k=K)

        weights_in = sem("weights_in")
        consts = sem("consts")
        w1_turned = sem("w1_turned")
        wa_done = sem("wa_done")
        w_hi_done = sem("w_hi_done")
        weights_ready = sem("weights_ready")
        def sems_of(**events_per_graph):
            return [sems(name) for name in events_per_graph]

        x_in, adj_in, out_stored, pen_ready, edge_ready = sems_of(
            x_in=DMA, adj_in=DMA, out_stored=DMA, pen_ready=2, edge_ready=1)
        pent_ps, pent_ready, deg_ps, deg_ready, stats_ready, mv_ready = sems_of(
            pent_ps=1, pent_ready=1, deg_ps=1, deg_ready=2, stats_ready=8, mv_ready=8)
        eps_ready, rstd_ready, xn_ready, ht_ps, hth_ready, htl_ready = sems_of(
            eps_ready=8, rstd_ready=8, xn_ready=16, ht_ps=10, hth_ready=10, htl_ready=10)
        other_ps, other_ready, wh_ps = sems_of(
            other_ps=3, other_ready=3, wh_ps=12)
        wh_ready, slope_ready, leaky_ready, q_ready, p_ready, inv_ready = sems_of(
            wh_ready=12, slope_ready=12, leaky_ready=12, q_ready=12, p_ready=12, inv_ready=12)
        scaled_ready, pt_ps, pt_ready, att_ps, relu_ready, elu_exp = sems_of(
            scaled_ready=4, pt_ps=8, pt_ready=8, att_ps=12, relu_ready=4, elu_exp=4)
        elu_clamped, elu_ready, x_ready, hh_ready, hl_ready, agg_ps = sems_of(
            elu_clamped=8, elu_ready=6, x_ready=16, hh_ready=4, hl_ready=4, agg_ps=4)
        agh_ready, agl_ready, root_ps, root_ready, rel_ps, u_ready = sems_of(
            agh_ready=4, agl_ready=4, root_ps=4, root_ready=4, rel_ps=4, u_ready=4)
        ce_ready, h1_ready = sems_of(
            ce_ready=4, h1_ready=4)

        def first(n):
            return isinstance(n, int) and n == 0

        def split3(pe, acc, pairs, last_stop=True, first=True):
            for i, (lh, ll, rh, rl) in enumerate(pairs):
                pe.matmul(acc, lh, rh, start=(first and i == 0), stop=False)
                pe.matmul(acc, lh, rl, start=False, stop=False)
                mm = pe.matmul(acc, ll, rh, start=False, stop=(last_stop and i == len(pairs) - 1))
            return mm

        def raw(i):
            tile = score[1] if i < 4 else prob[1]
            return tile[:, i % 4, :].rearrange("p (k o) -> p k o", k=K)

        W0, W1_RAW, W3, ROOT1, REL1, ROOT2, REL2, W1 = range(8)
        vectors = prob[0]
        bias_raw = prob[0][0:1, 3, :].rearrange("q (c d) -> q c d", c=2)
        scratch = h[1][:, 0, 0:D]

        block = ctx.enter_context(nc.Block())

        @block.sync
        def _(sp):
            def load_adj(s, n):
                sp.dma_start(adj_raw[s][:], adj[SLOTS * n + s].rearrange("(t p) j -> p t j", p=P))\
                    .then_inc(adj_in[s], DMA)

            def load_x(s, n):
                sp.dma_start(x_new[s][:], x[SLOTS * n + s].rearrange("(t p) d -> p t d", p=P))\
                    .then_inc(x_in[s], DMA)

            def store(s, n):
                sp.wait_ge(x_ready[s], 16 * n + 16)
                sp.dma_start(out[SLOTS * n + s].rearrange("(t p) d -> p t d", p=P), result[s])\
                    .then_inc(out_stored[s], DMA)

            load_adj(0, 0)
            load_x(0, 0)
            for i, w in enumerate((gat_w[0], gat_w[1], gat_w[2], conv_root[0], conv_rel[0][1],
                                   conv_root[1], conv_rel[1][1])):
                sp.dma_start(raw(i), w.rearrange("(k p) o -> p k o", p=P)).then_inc(weights_in, DMA)
            for i, a in enumerate(gat_a):
                sp.dma_start(vectors[:, i, :], a.rearrange("(q a) b -> q (a b)", q=1).to_broadcast([P, 2 * D]))\
                    .then_inc(weights_in, DMA)
            for c in range(2):
                sp.dma_start(bias_raw[:, c, :], conv_bias[c].rearrange("(q d) -> q d", q=1))\
                    .then_inc(weights_in, DMA)
            load_adj(1, 0)
            load_x(1, 0)
            with sp.Fori(0, ROUNDS - 1) as n:
                for s in range(SLOTS):
                    sp.wait_ge(edge_ready[s], n + 1)
                    load_adj(s, n + 1)
                    sp.wait_ge(x_ready[s], 16 * n + 4)
                    load_x(s, n + 1)
                for s in range(SLOTS):
                    store(s, n)
            for s in range(SLOTS):
                store(s, ROUNDS - 1)
            for s in range(SLOTS):
                sp.wait_ge(out_stored[s], DMA * ROUNDS)

        def run(eng, front, back, norm, conv):
            def segments(which, s, n, start):
                every = [lambda: front(s, 0, n), lambda: back(s, 0, n), lambda: front(s, 1, n),
                         lambda: back(s, 1, n), lambda: norm(s, n), lambda: conv(s, 0, n), lambda: conv(s, 1, n),
                         lambda: front(s, 3, n), lambda: back(s, 3, n)]
                return [(every[i](), [start + at for at in PLAN[i]]) for i in which]
            whole, early, late = range(len(PLAN)), range(HALFWAY), range(HALFWAY, len(PLAN))
            interleave(*segments(whole, 0, 0, 0), *segments(early, 1, 0, BEHIND))
            with eng.Fori(1, ROUNDS) as n:
                interleave(*segments(late, 1, n - 1, BEHIND - PERIOD), *segments(whole, 0, n, 0),
                           *segments(early, 1, n, BEHIND))
            interleave(*segments(late, 1, ROUNDS - 1, BEHIND))

        @block.gpsimd
        def _(pool):
            pool.memset(ident[:], 0.0).then_inc(consts, 1)
            pool.memset(ident16[:], 0.0).then_inc(consts, 1)
            pool.memset(ones_row[:].bitcast(F32), 1.0).then_inc(consts, 1)
            pool.memset(ones_col[:].bitcast(F32), 1.0).then_inc(consts, 1)
            pool.memset(half_t[:], -0.5).then_inc(consts, 1)
            pool.wait_ge(consts, 5)
            for m in (ident, ident16):
                pool.affine_select(out=m[:], in_=m[:], compare_op=ALU.not_equal, fill=1.0, base=0,
                                   pattern=[[-1, P]], channel_multiplier=1).then_inc(consts, 1)

            def rstd_of(s, layer, half, n):
                two = slice(2 * half, 2 * half + 2)
                pool.wait_ge(eps_ready[s], 8 * n + 2 * layer + half + 1)
                pool.tensor_tensor(rstd[s][:, two], var_eps[s][:, two], half_t[:, two], ALU.pow)\
                    .then_inc(rstd_ready[s], 1)

            def front(s, layer, n):
                rstd_of(s, layer, 0, n)
                yield
                rstd_of(s, layer, 1, n)
                for _ in PLAN[SEGMENTS.index("front")][1:]:
                    yield

            def norm(s, n):
                rstd_of(s, 2, 0, n)
                yield
                rstd_of(s, 2, 1, n)
                yield

            def back(s, layer, n):
                for what, t in BACK_STEPS[layer]:
                    if what == "out" and layer == 0:
                        pool.wait_ge(relu_ready[s], 4 * n + t + 1)
                        pool.tensor_tensor(xs[s][:, t, :], x_new[s][:, t, :], score[s][:, t, 0:D], ALU.add)\
                            .then_inc(x_ready[s], 1)
                    elif what == "out" and layer == 3:
                        pool.wait_ge(elu_ready[s], 6 * n + 2 + t + 1)
                        pool.tensor_tensor(result[s][:, t, :], xs[s][:, t, :], score[s][:, t, 0:D], ALU.add)\
                            .then_inc(x_ready[s], 1)
                    yield

            def conv(s, c, n):
                yield
                for half in range(2):
                    if c == 1:
                        two = slice(2 * half, 2 * half + 2)
                        pool.wait_ge(hh_ready[s], 4 * n + 2 * c + half + 1)
                        pool.tensor_tensor(h_lo[s][:, two, :], h[s][:, two, 0:D], h_hi[s][:, two, :].bitcast(F32),
                                           ALU.subtract).then_inc(hl_ready[s], 1)
                    yield
                for _ in range(4):
                    yield
                for half in range(2):
                    if c == 1:
                        pool.wait_ge(elu_ready[s], 6 * n + half + 1)
                        for i in range(2):
                            t = 2 * half + i
                            pool.tensor_tensor(xs[s][:, t, :], xs[s][:, t, :], prob[s][:, half, i * D:(i + 1) * D],
                                               ALU.add).then_inc(x_ready[s], 1)
                    yield

            run(pool, front, back, norm, conv)

        @block.scalar
        def _(act):
            act.wait_ge(consts, 7)

            def turned_hi(s, turn, half, n, what):
                nodes = slice(half * 2 * P, (half + 1) * 2 * P)
                act.wait_ge(ht_ps[s], 10 * n + 2 * turn + half + 1)
                act.activation(ht_hi[s][:, :, nodes], turned(s, half), what).then_inc(hth_ready[s], 1)

            def front(s, layer, n):
                g = GAT_OF_LAYER[layer]
                turn = {0: 0, 1: 1, 3: 4}[layer]
                yield
                yield
                turned_hi(s, turn, 0, n, ACT.Relu)
                yield
                turned_hi(s, turn, 1, n, ACT.Relu)
                yield
                if layer == 0:
                    act.wait_ge(pent_ps[s], n + 1)
                    act.activation(pen_turned[s][:], ps[s][:, 2:4, :].bitcast(BF16).rearrange(
                        "p b (t i) -> p (b t) i", t=2), ACT.Copy).then_inc(pent_ready[s], 1)
                yield
                act.wait_ge(other_ps[s], 3 * n + g + 1)
                act.activation(other(s), ps[s][:, 2, :], ACT.Copy).then_inc(other_ready[s], 1)
                yield

            def back(s, layer, n):
                g = GAT_OF_LAYER[layer]
                for what, t in BACK_STEPS[layer]:
                    e = 12 * n + 4 * g + t + 1
                    if what == "values":
                        act.wait_ge(wh_ps[s], e)
                        act.activation(h[s][:, t, :], ps[s][:, BANK[t], 0:WS], ACT.Copy).then_inc(wh_ready[s], 1)
                    elif what == "score":
                        if t == 0:
                            act.wait_ge(other_ready[s], 3 * n + g + 1)
                        act.wait_ge(wh_ready[s], e)
                        act.activation(prob[s][:, t, :], other(s), ACT.Identity, scale=SLOPE,
                                       bias=h[s][:, t, OWN_SLOPE:OWN_SLOPE + 1]).then_inc(slope_ready[s], 1)
                    elif what == "exp":
                        act.wait_ge(q_ready[s], e)
                        act.activation(prob[s][:, t, :], score[s][:, t, :], ACT.Exp, scale=-1.0,
                                       bias=neg_max[s][:, t:t + 1], accum_out=row_sum[s][:, t:t + 1])\
                            .then_inc(p_ready[s], 1)
                    elif what == "copy" and layer != 3:
                        act.wait_ge(pt_ps[s], 8 * n + 4 * g + t + 1)
                        act.activation(turned_prob[s][:, t, :], ps[s][:, BANK[t], :], ACT.Copy).then_inc(pt_ready[s], 1)
                    elif what == "out" and layer == 0:
                        act.wait_ge(inv_ready[s], e)
                        act.wait_ge(att_ps[s], e)
                        act.activation(score[s][:, t, 0:D], ps[s][:, BANK[t], 0:D], ACT.Relu,
                                       scale=inv_sum[s][:, t:t + 1]).then_inc(relu_ready[s], 1)
                    elif what == "out" and layer == 3:
                        act.wait_ge(att_ps[s], e)
                        act.activation(score[s][:, t, 0:D], ps[s][:, BANK[t], 0:D], ACT.Exp).then_inc(elu_exp[s], 1)
                    yield

            def norm(s, n):
                yield
                yield

            def conv(s, c, n):
                what = ACT.Copy if c else ACT.Relu
                for half in range(2):
                    two = slice(2 * half, 2 * half + 2)
                    turned_hi(s, 2 + c, half, n, what)
                    act.activation(h_hi[s][:, two, :], h[s][:, two, 0:D], what).then_inc(hh_ready[s], 1)
                    yield
                for k in range(K):
                    act.wait_ge(agg_ps[s], 4 * n + 2 * c + k + 1)
                    act.activation(sum_hi[s][:, k, :], ps[s][:, 2 + k, :], ACT.Copy).then_inc(agh_ready[s], 1)
                    yield
                for half in range(2):
                    act.wait_ge(root_ps[s], 4 * n + 2 * c + half + 1)
                    act.activation(score[s][:, half, :], ps[s][:, half, :], ACT.Copy).then_inc(root_ready[s], 1)
                    yield
                for half in range(2):
                    act.wait_ge(u_ready[s], 4 * n + 2 * c + half + 1)
                    act.activation(prob[s][:, half, :], score[s][:, 2 + half, :], ACT.Exp).then_inc(ce_ready[s], 1)
                    yield
                yield

            run(act, front, back, norm, conv)

        @block.vector
        def _(dve):
            dve.wait_ge(weights_in, 12 * DMA)
            dve.wait_ge(w1_turned, 1)
            dve.tensor_copy(raw(W1), ps[0][:, 0:K, 0:D]).then_inc(wa_done, 1)
            dve.wait_ge(wa_done, 1)
            count = 1
            for g, w in enumerate((W0, W1, W3)):
                for k in range(K):
                    for c in range(2):
                        a = 1 - c if g == 2 else c
                        dve.tensor_tensor_reduce(scratch, raw(w)[:, k, :], vectors[:, g, a * D:(a + 1) * D],
                                                 1.0, 0.0, ALU.mult, ALU.add, wa[:, g, k, c:c + 1])\
                            .then_inc(wa_done, 1)
                        count += 1
                        dve.wait_ge(wa_done, count)
            dve.tensor_scalar(wa[:, :, :, 2:4], wa[:, :, :, 0:2], SLOPE, None, ALU.mult).then_inc(wa_done, 1)
            dve.wait_ge(wa_done, count + 1)
            splits = []
            for g, w in enumerate((W0, W1, W3)):
                splits.append((wg_hi[g][:, :, 0:D], wg_lo[g][:, :, 0:D], raw(w)))
                splits.append((wg_hi[g][:, :, D:WS], wg_lo[g][:, :, D:WS], wa[:, g, :, :]))
            for i, w in enumerate((ROOT1, REL1, ROOT2, REL2)):
                splits.append((wc_hi[i][:], wc_lo[i][:], raw(w)))
            splits.append((bias_hi[:], bias_lo[:], bias_raw[:]))
            for hi, _, full in splits:
                dve.tensor_copy(hi, full).then_inc(w_hi_done, 1)
            dve.wait_ge(w_hi_done, len(splits))
            for hi, lo, full in splits:
                dve.tensor_tensor(lo, full, hi.bitcast(F32), ALU.subtract).then_inc(weights_ready, 1)
            assert len(splits) == N_SPLITS

            def statistics(s, layer, half, n):
                for t in (2 * half, 2 * half + 1):
                    if layer == 0:
                        dve.wait_ge(x_in[s], DMA * (n + 1))
                    else:
                        dve.wait_ge(x_ready[s], 16 * n + 4 * (layer - 1) + t + 1)
                    source = x_new if layer == 0 else xs
                    st = dve.bn_stats(stats[s][:, t, :], source[s][:, t, :])
                st.then_inc(stats_ready[s], 1)
                dve.wait_ge(stats_ready[s], 8 * n + 2 * layer + half + 1)
                dve.memset(settled[:], 0.0)
                for t in (2 * half, 2 * half + 1):
                    agg = dve.bn_aggr(mean_var[s][:, t, :], stats[s][:, t, :])
                agg.then_inc(mv_ready[s], 1)
                two = slice(2 * half, 2 * half + 2)
                dve.wait_ge(mv_ready[s], 8 * n + 2 * layer + half + 1)
                dve.tensor_scalar(var_eps[s][:, two], mean_var[s][:, two, 1], EPS, None, ALU.add)\
                    .then_inc(eps_ready[s], 1)

            def normalised(s, layer, half, n):
                dve.wait_ge(rstd_ready[s], 8 * n + 2 * layer + half + 1)
                for t in (2 * half, 2 * half + 1):
                    source = x_new if layer == 0 else xs
                    dve.tensor_scalar(h[s][:, t, 0:D], source[s][:, t, :], mean_var[s][:, t, 0:1], rstd[s][:, t:t + 1],
                                      ALU.subtract, ALU.mult).then_inc(xn_ready[s], 1)

            def turned_lo(s, turn, half, n, relu=True):
                nodes = slice(half * 2 * P, (half + 1) * 2 * P)
                dve.wait_ge(hth_ready[s], 10 * n + 2 * turn + half + 1)
                lo, hi = ht_lo[s][:, :, nodes], ht_hi[s][:, :, nodes].bitcast(F32)
                if relu:
                    dve.scalar_tensor_tensor(out=lo, in0=turned(s, half), scalar=0.0, in1=hi, op0=ALU.max,
                                             op1=ALU.subtract).then_inc(htl_ready[s], 1)
                else:
                    dve.tensor_tensor(lo, turned(s, half), hi, ALU.subtract).then_inc(htl_ready[s], 1)

            def front(s, layer, n):
                g = GAT_OF_LAYER[layer]
                turn = {0: 0, 1: 1, 3: 4}[layer]
                statistics(s, layer, 0, n)
                yield
                statistics(s, layer, 1, n)
                if layer == 0:
                    dve.wait_ge(adj_in[s], DMA * (n + 1))
                    dve.tensor_scalar(pen[s][:], adj_raw[s][:], 0.0, MASKED, ALU.is_le, ALU.mult)\
                        .then_inc(pen_ready[s], 1)
                normalised(s, layer, 0, n)
                yield
                normalised(s, layer, 1, n)
                yield
                turned_lo(s, turn, 0, n)
                yield
                turned_lo(s, turn, 1, n)
                yield
                if layer == 1:
                    dve.wait_ge(deg_ps[s], n + 1)
                    dve.tensor_scalar(degree[s][:], ps[s][:, 3, 0:2 * T].rearrange("p (t two) -> p t two", two=2)[:, :, 0],
                                      1.0, None, ALU.max).then_inc(deg_ready[s], 1)
                    dve.wait_ge(deg_ready[s], 2 * n + 1)
                    dve.reciprocal(inv_degree[s][:], degree[s][:]).then_inc(deg_ready[s], 1)
                yield

            def back(s, layer, n):
                g = GAT_OF_LAYER[layer]
                penalties = pen_turned if layer == 3 else pen
                for what, t in BACK_STEPS[layer]:
                    e = 12 * n + 4 * g + t + 1
                    if what == "score":
                        if t == 0:
                            if layer == 3:
                                dve.wait_ge(pent_ready[s], n + 1)
                            else:
                                dve.wait_ge(pen_ready[s], 2 * n + g + 1)
                            if layer == 0 and not first(n):
                                dve.wait_ge(out_stored[s], DMA * n)
                        dve.wait_ge(slope_ready[s], e)
                        dve.scalar_tensor_tensor(out=prob[s][:, t, :], in0=other(s),
                                                 scalar=h[s][:, t, OWN:OWN + 1], in1=prob[s][:, t, :],
                                                 op0=ALU.add, op1=ALU.max).then_inc(leaky_ready[s], 1)
                        dve.wait_ge(leaky_ready[s], e)
                        dve.memset(settled[:], 0.0)
                        dve.tensor_tensor_reduce(score[s][:, t, :], prob[s][:, t, :], penalties[s][:, t, :],
                                                 -1.0, -LOWEST, ALU.add, ALU.min, neg_max[s][:, t:t + 1])\
                            .then_inc(q_ready[s], 1)
                    elif what == "copy":
                        dve.wait_ge(p_ready[s], e)
                        dve.reciprocal(inv_sum[s][:, t:t + 1], row_sum[s][:, t:t + 1]).then_inc(inv_ready[s], 1)
                        if layer == 3:
                            dve.wait_ge(inv_ready[s], e)
                            dve.tensor_scalar(h[s][:, t, 0:D], h[s][:, t, 0:D], inv_sum[s][:, t:t + 1], None, ALU.mult)\
                                .then_inc(scaled_ready[s], 1)
                        if layer == 0 and t == 3:
                            dve.wait_ge(pent_ps[s], n + 1)
                            dve.wait_ge(q_ready[s], 12 * n + 4)
                            dve.tensor_scalar(pen[s][:], adj_raw[s][:], 0.0, MASKED, ALU.is_equal, ALU.mult)\
                                .then_inc(pen_ready[s], 1)
                    elif what == "product" and layer == 0 and t == 3:
                        dve.tensor_scalar(edge[s][:], adj_raw[s][:], 1.0, None, ALU.is_equal).then_inc(edge_ready[s], 1)
                    elif what == "out" and layer == 1:
                        dve.wait_ge(inv_ready[s], e)
                        dve.wait_ge(att_ps[s], e)
                        dve.scalar_tensor_tensor(out=xs[s][:, t, :], in0=ps[s][:, BANK[t], 0:D],
                                                 scalar=inv_sum[s][:, t:t + 1], in1=xs[s][:, t, :],
                                                 op0=ALU.mult, op1=ALU.add).then_inc(x_ready[s], 1)
                    elif what == "out" and layer == 3:
                        y = score[s][:, t, 0:D]
                        dve.wait_ge(elu_exp[s], 4 * n + t + 1)
                        dve.tensor_scalar(y, y, 1.0, -1.0, ALU.min, ALU.add).then_inc(elu_clamped[s], 1)
                        dve.wait_ge(elu_clamped[s], 8 * n + 4 + t + 1)
                        dve.tensor_tensor(y, ps[s][:, BANK[t], 0:D], y, ALU.max).then_inc(elu_ready[s], 1)
                    yield

            def norm(s, n):
                statistics(s, 2, 0, n)
                yield
                statistics(s, 2, 1, n)
                normalised(s, 2, 0, n)
                normalised(s, 2, 1, n)
                yield

            def conv(s, c, n):
                yield
                for half in range(2):
                    turned_lo(s, 2 + c, half, n, relu=(c == 0))
                    if c == 0:
                        two = slice(2 * half, 2 * half + 2)
                        dve.wait_ge(hh_ready[s], 4 * n + half + 1)
                        dve.scalar_tensor_tensor(out=h_lo[s][:, two, :], in0=h[s][:, two, 0:D], scalar=0.0,
                                                 in1=h_hi[s][:, two, :].bitcast(F32), op0=ALU.max, op1=ALU.subtract)\
                            .then_inc(hl_ready[s], 1)
                    yield
                for k in range(K):
                    dve.wait_ge(agh_ready[s], 4 * n + 2 * c + k + 1)
                    dve.tensor_tensor(sum_lo[s][:, k, :], ps[s][:, 2 + k, :], sum_hi[s][:, k, :].bitcast(F32),
                                      ALU.subtract).then_inc(agl_ready[s], 1)
                    yield
                yield
                for half in range(3):
                    if half < 2:
                        dve.wait_ge(root_ready[s], 4 * n + 2 * c + half + 1)
                        dve.wait_ge(rel_ps[s], 4 * n + 2 * c + half + 1)
                        for i in range(2):
                            t = 2 * half + i
                            u = dve.scalar_tensor_tensor(
                                out=score[s][:, 2 + half, i * D:(i + 1) * D],
                                in0=ps[s][:, 2 + half, i * D:(i + 1) * D], scalar=inv_degree[s][:, t:t + 1],
                                in1=score[s][:, half, i * D:(i + 1) * D], op0=ALU.mult, op1=ALU.add)
                        u.then_inc(u_ready[s], 1)
                    if half > 0:
                        b = half - 1
                        y = prob[s][:, b, :]
                        dve.wait_ge(ce_ready[s], 4 * n + 2 * c + b + 1)
                        dve.tensor_scalar(y, y, 1.0, -1.0, ALU.min, ALU.add).then_inc(elu_clamped[s], 1)
                        dve.wait_ge(elu_clamped[s], 8 * n + 2 * c + b + 1)
                        if c == 0:
                            for i in range(2):
                                dve.tensor_tensor(h[s][:, 2 * b + i, 0:D], score[s][:, 2 + b, i * D:(i + 1) * D],
                                                  y[:, i * D:(i + 1) * D], ALU.max).then_inc(h1_ready[s], 1)
                        else:
                            dve.tensor_tensor(y, score[s][:, 2 + b, :], y, ALU.max).then_inc(elu_ready[s], 1)
                    yield

            run(dve, front, back, norm, conv)

        @block.tensor
        def _(pe):
            pe.wait_ge(consts, 7)
            pe.wait_ge(weights_in, 12 * DMA)
            for k in range(K):
                for o in range(K):
                    mm = pe.transpose(ps[0][:, k, o * P:(o + 1) * P], raw(W1_RAW)[:, o, k * P:(k + 1) * P], ident[:])
            mm.then_inc(w1_turned, 1)
            pe.wait_ge(weights_ready, N_SPLITS)

            def turn_h(s, turn, half, n):
                for t in (2 * half, 2 * half + 1):
                    if turn == 3:
                        pe.wait_ge(h1_ready[s], 4 * n + t + 1)
                    else:
                        pe.wait_ge(xn_ready[s], 16 * n + 4 * {0: 0, 1: 1, 2: 2, 4: 3}[turn] + t + 1)
                    for k in range(K):
                        mm = pe.transpose(turned(s, half)[:, k, (t % 2) * P:(t % 2 + 1) * P], h[s][:, t, k * P:(k + 1) * P],
                                          ident[:])
                mm.then_inc(ht_ps[s], 1)

            def front(s, layer, n):
                g = GAT_OF_LAYER[layer]
                turn = {0: 0, 1: 1, 3: 4}[layer]
                if layer == 0 and not first(n):
                    pe.wait_ge(x_ready[s], 16 * n)
                if layer == 1:
                    pe.wait_ge(edge_ready[s], n + 1)
                    pe.wait_ge(x_ready[s], 16 * n + 1)
                    for j in range(T):
                        for i in range(T):
                            mm = pe.matmul(ps[s][:, 3, 2 * j:2 * j + 2], edge[s][:, i, j * P:(j + 1) * P],
                                           ones_col[:], start=(i == 0), stop=(i == T - 1))
                    mm.then_inc(deg_ps[s], 1)
                yield
                if layer == 0:
                    pe.wait_ge(pen_ready[s], 2 * n + 1)
                    turned_pen = ps[s][:, 2:4, :].bitcast(BF16).rearrange("p b (t i) -> p (b t) i", t=2)
                    for j in range(T):
                        for i in range(T):
                            mm = pe.transpose(turned_pen[:, j, i * P:(i + 1) * P], pen[s][:, i, j * P:(j + 1) * P], ident16[:])
                    mm.then_inc(pent_ps[s], 1)
                yield
                turn_h(s, turn, 0, n)
                yield
                turn_h(s, turn, 1, n)
                yield
                for half in range(2):
                    pe.wait_ge(hth_ready[s], 10 * n + 2 * turn + half + 1)
                    pe.wait_ge(htl_ready[s], 10 * n + 2 * turn + half + 1)
                    if layer == 0 and half == 0:
                        pe.wait_ge(pent_ready[s], n + 1)
                    c = slice(half * 2 * P, (half + 1) * 2 * P)
                    mm = split3(pe, ps[s][:, 2, c],
                                [(wg_hi[g][:, k, OTHER:OTHER + 1].to_broadcast([P, P]),
                                  wg_lo[g][:, k, OTHER:OTHER + 1].to_broadcast([P, P]),
                                  ht_hi[s][:, k, c], ht_lo[s][:, k, c]) for k in range(K)])
                    if half == 1:
                        mm.then_inc(other_ps[s], 1)
                    yield

            def back(s, layer, n):
                g = GAT_OF_LAYER[layer]
                for what, t in BACK_STEPS[layer]:
                    e = 12 * n + 4 * g + t + 1
                    if what == "values":
                        if t == 0 and layer == 1:
                            pe.wait_ge(deg_ready[s], 2 * n + 1)
                        if t == 3:
                            pe.wait_ge(other_ready[s], 3 * n + g + 1)
                        c = slice(t * P, (t + 1) * P)
                        split3(pe, ps[s][:, BANK[t], 0:WS],
                               [(ht_hi[s][:, k, c], ht_lo[s][:, k, c], wg_hi[g][:, k, :], wg_lo[g][:, k, :])
                                for k in range(K)]).then_inc(wh_ps[s], 1)
                    elif what == "exp" and layer != 3:
                        pe.wait_ge(p_ready[s], e)
                        for j in range(T):
                            mm = pe.transpose(ps[s][:, BANK[t], j * P:(j + 1) * P], prob[s][:, t, j * P:(j + 1) * P],
                                              ident[:])
                        mm.then_inc(pt_ps[s], 1)
                    elif what == "product":
                        if layer == 3:
                            pe.wait_ge(scaled_ready[s], 4 * n + 4)
                            pe.wait_ge(p_ready[s], 12 * n + 4 * g + 4)
                        else:
                            pe.wait_ge(pt_ready[s], 8 * n + 4 * g + t + 1)
                        for j in range(T):
                            if layer == 3:
                                weights = prob[s][:, j, t * P:(t + 1) * P]
                            else:
                                weights = turned_prob[s][:, t, j * P:(j + 1) * P]
                            mm = pe.matmul(ps[s][:, BANK[t], 0:D], weights, h[s][:, j, 0:D], start=(j == 0),
                                           stop=(j == T - 1))
                        mm.then_inc(att_ps[s], 1)
                    yield

            def norm(s, n):
                yield
                yield

            def conv(s, c, n):
                turn_h(s, 2 + c, 0, n)
                yield
                turn_h(s, 2 + c, 1, n)
                yield
                for k in range(K):
                    if k == 0:
                        pe.wait_ge(hh_ready[s], 4 * n + 2 * c + 2)
                        pe.wait_ge(hl_ready[s], 4 * n + 2 * c + 2)
                    for i, part in enumerate((h_hi, h_lo)):
                        for t in range(T):
                            mm = pe.matmul(ps[s][:, 2 + k, :], part[s][:, t, k * P:(k + 1) * P], edge[s][:, t, :],
                                           start=(i == 0 and t == 0), stop=(i == 1 and t == T - 1))
                    mm.then_inc(agg_ps[s], 1)
                    yield
                for half in range(2):
                    pe.wait_ge(hth_ready[s], 10 * n + 2 * (2 + c) + 2)
                    pe.wait_ge(htl_ready[s], 10 * n + 2 * (2 + c) + 2)
                    for i in range(2):
                        t = 2 * half + i
                        cols = slice(t * P, (t + 1) * P)
                        acc = ps[s][:, half, i * D:(i + 1) * D]
                        split3(pe, acc, [(ht_hi[s][:, k, cols], ht_lo[s][:, k, cols],
                                          wc_hi[2 * c][:, k, :], wc_lo[2 * c][:, k, :]) for k in range(K)],
                               last_stop=False)
                        pe.matmul(acc, ones_row[:], bias_hi[:, c, :], start=False, stop=False)
                        mm = pe.matmul(acc, ones_row[:], bias_lo[:, c, :], start=False, stop=True)
                    mm.then_inc(root_ps[s], 1)
                    yield
                for half in range(2):
                    pe.wait_ge(agh_ready[s], 4 * n + 2 * c + 2)
                    pe.wait_ge(agl_ready[s], 4 * n + 2 * c + 2)
                    for i in range(2):
                        t = 2 * half + i
                        cols = slice(t * P, (t + 1) * P)
                        mm = split3(pe, ps[s][:, 2 + half, i * D:(i + 1) * D],
                                    [(sum_hi[s][:, k, cols], sum_lo[s][:, k, cols],
                                      wc_hi[2 * c + 1][:, k, :], wc_lo[2 * c + 1][:, k, :]) for k in range(K)])
                    mm.then_inc(rel_ps[s], 1)
                    yield
                yield

            run(pe, front, back, norm, conv)


_INS = ["x", "adj", "L0_gnn_W", "L0_gnn_a", "L1_gnn_W", "L1_gnn_a", "L2_gnn_w_rel1", "L2_gnn_w_root1",
        "L2_gnn_b1", "L2_gnn_w_rel2", "L2_gnn_w_root2", "L2_gnn_b2", "L3_gnn_W", "L3_gnn_a"]


def kernel(**inputs):
    import numpy as _np
    import concourse.bacc as _bacc
    from concourse.bass_utils import run_bass_kernel_spmd as _run

    nc = _bacc.Bacc("TRN2", target_bir_lowering=False, num_devices=1)
    arrays, a = {}, {}
    for name in _INS:
        v = _np.ascontiguousarray(inputs[name])
        arrays[name] = v
        a[name] = nc.dram_tensor(name, v.shape, mybir.dt.from_np(v.dtype), kind="ExternalInput").ap()
    out = nc.dram_tensor("out", inputs["x"].shape, F32, kind="ExternalOutput").ap()
    build(nc, a["x"], a["adj"], [a["L0_gnn_W"], a["L1_gnn_W"], a["L3_gnn_W"]],
          [a["L0_gnn_a"], a["L1_gnn_a"], a["L3_gnn_a"]],
          [a["L2_gnn_w_rel1"], a["L2_gnn_w_rel2"]], [a["L2_gnn_w_root1"], a["L2_gnn_w_root2"]],
          [a["L2_gnn_b1"], a["L2_gnn_b2"]], out)
    r = _run(nc, [arrays], core_ids=[0])
    return r.results[0]["out"]
```
